# Optimizing a Trainium2 kernel written in Bass

```python
import numpy as np
import jax
import jax.numpy as jnp

def _softmax(x, axis=-1):
    return jax.nn.softmax(x, axis=axis)

def _gelu(x):
    return jax.nn.gelu(x, approximate=True)

def _silu(x):
    return jax.nn.silu(x)

def _sigmoid(x):
    return jax.nn.sigmoid(x)

def _layernorm(x, axis=-1, eps=1e-05):
    m = jnp.mean(x, axis=axis, keepdims=True)
    v = jnp.var(x, axis=axis, keepdims=True)
    return (x - m) / jnp.sqrt(v + eps)

def _scatter_add(tgt, idx, src, axis=0):
    return tgt.at[idx].add(src)

def _segment_sum(src, seg, n):
    return jax.ops.segment_sum(src, seg, n)
kernel_name = 'mk_dlrm_tower_d1_rec_r8_4c12be'

def setup_inputs(seed: int=0):
    np.random.seed(seed)
    _w = jnp.asarray

    def _rec_inputs():
        import jax
        import jax.numpy as jnp
        _tk = jax.random.key(seed)
        ids = jnp.stack([jax.random.randint(jax.random.fold_in(_tk, 200 + f), (2048,), 0, v, jnp.int32) for f, v in enumerate([125000, 1250, 1000, 1250, 1250, 1000, 1250, 12500, 1000, 12500, 1000, 1250, 1000, 1000, 12500, 1250, 1000, 12500, 1250, 1000, 12500, 1000, 1000, 1250, 12500, 1250])], axis=1)
        tbl_0 = 0.05 * jax.random.normal(jax.random.fold_in(_tk, 500 + 0), (125000, 128), jnp.float32)
        tbl_1 = 0.05 * jax.random.normal(jax.random.fold_in(_tk, 500 + 1), (1250, 128), jnp.float32)
        tbl_2 = 0.05 * jax.random.normal(jax.random.fold_in(_tk, 500 + 2), (1000, 128), jnp.float32)
        tbl_3 = 0.05 * jax.random.normal(jax.random.fold_in(_tk, 500 + 3), (1250, 128), jnp.float32)
        tbl_4 = 0.05 * jax.random.normal(jax.random.fold_in(_tk, 500 + 4), (1250, 128), jnp.float32)
        tbl_5 = 0.05 * jax.random.normal(jax.random.fold_in(_tk, 500 + 5), (1000, 128), jnp.float32)
        tbl_6 = 0.05 * jax.random.normal(jax.random.fold_in(_tk, 500 + 6), (1250, 128), jnp.float32)
        tbl_7 = 0.05 * jax.random.normal(jax.random.fold_in(_tk, 500 + 7), (12500, 128), jnp.float32)
        tbl_8 = 0.05 * jax.random.normal(jax.random.fold_in(_tk, 500 + 8), (1000, 128), jnp.float32)
        tbl_9 = 0.05 * jax.random.normal(jax.random.fold_in(_tk, 500 + 9), (12500, 128), jnp.float32)
        tbl_10 = 0.05 * jax.random.normal(jax.random.fold_in(_tk, 500 + 10), (1000, 128), jnp.float32)
        tbl_11 = 0.05 * jax.random.normal(jax.random.fold_in(_tk, 500 + 11), (1250, 128), jnp.float32)
        tbl_12 = 0.05 * jax.random.normal(jax.random.fold_in(_tk, 500 + 12), (1000, 128), jnp.float32)
        tbl_13 = 0.05 * jax.random.normal(jax.random.fold_in(_tk, 500 + 13), (1000, 128), jnp.float32)
        tbl_14 = 0.05 * jax.random.normal(jax.random.fold_in(_tk, 500 + 14), (12500, 128), jnp.float32)
        tbl_15 = 0.05 * jax.random.normal(jax.random.fold_in(_tk, 500 + 15), (1250, 128), jnp.float32)
        tbl_16 = 0.05 * jax.random.normal(jax.random.fold_in(_tk, 500 + 16), (1000, 128), jnp.float32)
        tbl_17 = 0.05 * jax.random.normal(jax.random.fold_in(_tk, 500 + 17), (12500, 128), jnp.float32)
        tbl_18 = 0.05 * jax.random.normal(jax.random.fold_in(_tk, 500 + 18), (1250, 128), jnp.float32)
        tbl_19 = 0.05 * jax.random.normal(jax.random.fold_in(_tk, 500 + 19), (1000, 128), jnp.float32)
        tbl_20 = 0.05 * jax.random.normal(jax.random.fold_in(_tk, 500 + 20), (12500, 128), jnp.float32)
        tbl_21 = 0.05 * jax.random.normal(jax.random.fold_in(_tk, 500 + 21), (1000, 128), jnp.float32)
        tbl_22 = 0.05 * jax.random.normal(jax.random.fold_in(_tk, 500 + 22), (1000, 128), jnp.float32)
        tbl_23 = 0.05 * jax.random.normal(jax.random.fold_in(_tk, 500 + 23), (1250, 128), jnp.float32)
        tbl_24 = 0.05 * jax.random.normal(jax.random.fold_in(_tk, 500 + 24), (12500, 128), jnp.float32)
        tbl_25 = 0.05 * jax.random.normal(jax.random.fold_in(_tk, 500 + 25), (1250, 128), jnp.float32)
        _rk = jax.random.fold_in(_tk, 7)
        r_bottom_output = -0.000520686 + 1.00062 * jax.random.normal(jax.random.fold_in(_rk, 101), (2048, 128), jnp.float32)
        W_top1 = 0.0456912 * jax.random.normal(jax.random.fold_in(_tk, 801), (479, 512), jnp.float32)
        W_top2 = 0.0441942 * jax.random.normal(jax.random.fold_in(_tk, 802), (512, 256), jnp.float32)
        W_top3 = 0.0625 * jax.random.normal(jax.random.fold_in(_tk, 803), (256, 1), jnp.float32)
        b_top1 = jnp.zeros((512,), jnp.float32)
        b_top2 = jnp.zeros((256,), jnp.float32)
        return (r_bottom_output, ids, tbl_0, tbl_1, tbl_2, tbl_3, tbl_4, tbl_5, tbl_6, tbl_7, tbl_8, tbl_9, tbl_10, tbl_11, tbl_12, tbl_13, tbl_14, tbl_15, tbl_16, tbl_17, tbl_18, tbl_19, tbl_20, tbl_21, tbl_22, tbl_23, tbl_24, tbl_25, W_top1, b_top1, W_top2, b_top2, W_top3)
    r_bottom_output, ids, tbl_0, tbl_1, tbl_2, tbl_3, tbl_4, tbl_5, tbl_6, tbl_7, tbl_8, tbl_9, tbl_10, tbl_11, tbl_12, tbl_13, tbl_14, tbl_15, tbl_16, tbl_17, tbl_18, tbl_19, tbl_20, tbl_21, tbl_22, tbl_23, tbl_24, tbl_25, W_top1, b_top1, W_top2, b_top2, W_top3 = _rec_inputs()

    def _L0_rec_setup():
        import jax, jax.numpy as jnp
        import numpy as np
        NUM_FEATURES = 27
        _TRIU_I, _TRIU_J = np.triu_indices(NUM_FEATURES, k=1)
        key = jax.random.key(seed)
        k1, k2 = jax.random.split(key)
        bottom_output = jax.random.normal(k1, (2048, 128), dtype=jnp.float32)
        embeddings = jax.random.normal(k2, (2048, 26, 128), dtype=jnp.float32)
        return {'bottom_output': bottom_output, 'embeddings': embeddings}
    _L0_rec_all = _L0_rec_setup()
    _L0_rec_in = {k: v for k, v in _L0_rec_all.items() if k in ()}
    del _L0_rec_all
    return {'r_bottom_output': r_bottom_output, 'ids': ids, 'tbl_0': tbl_0, 'tbl_1': tbl_1, 'tbl_2': tbl_2, 'tbl_3': tbl_3, 'tbl_4': tbl_4, 'tbl_5': tbl_5, 'tbl_6': tbl_6, 'tbl_7': tbl_7, 'tbl_8': tbl_8, 'tbl_9': tbl_9, 'tbl_10': tbl_10, 'tbl_11': tbl_11, 'tbl_12': tbl_12, 'tbl_13': tbl_13, 'tbl_14': tbl_14, 'tbl_15': tbl_15, 'tbl_16': tbl_16, 'tbl_17': tbl_17, 'tbl_18': tbl_18, 'tbl_19': tbl_19, 'tbl_20': tbl_20, 'tbl_21': tbl_21, 'tbl_22': tbl_22, 'tbl_23': tbl_23, 'tbl_24': tbl_24, 'tbl_25': tbl_25, 'W_top1': W_top1, 'b_top1': b_top1, 'W_top2': W_top2, 'b_top2': b_top2, 'W_top3': W_top3}

def reference(r_bottom_output, ids, tbl_0, tbl_1, tbl_2, tbl_3, tbl_4, tbl_5, tbl_6, tbl_7, tbl_8, tbl_9, tbl_10, tbl_11, tbl_12, tbl_13, tbl_14, tbl_15, tbl_16, tbl_17, tbl_18, tbl_19, tbl_20, tbl_21, tbl_22, tbl_23, tbl_24, tbl_25, W_top1, b_top1, W_top2, b_top2, W_top3):
    import jax
    import jax.numpy as jnp

    def _L0_rec_ref(bottom_output, embeddings):
        import jax, jax.numpy as jnp
        import numpy as np
        NUM_FEATURES = 27
        _TRIU_I, _TRIU_J = np.triu_indices(NUM_FEATURES, k=1)
        all_emb = jnp.concatenate([bottom_output[:, None, :], embeddings], axis=1)
        gram = jnp.einsum('bfd,bgd->bfg', all_emb, all_emb)
        return gram[:, _TRIU_I, _TRIU_J]
    e = jnp.stack([tbl_0[ids[:, 0]], tbl_1[ids[:, 1]], tbl_2[ids[:, 2]], tbl_3[ids[:, 3]], tbl_4[ids[:, 4]], tbl_5[ids[:, 5]], tbl_6[ids[:, 6]], tbl_7[ids[:, 7]], tbl_8[ids[:, 8]], tbl_9[ids[:, 9]], tbl_10[ids[:, 10]], tbl_11[ids[:, 11]], tbl_12[ids[:, 12]], tbl_13[ids[:, 13]], tbl_14[ids[:, 14]], tbl_15[ids[:, 15]], tbl_16[ids[:, 16]], tbl_17[ids[:, 17]], tbl_18[ids[:, 18]], tbl_19[ids[:, 19]], tbl_20[ids[:, 20]], tbl_21[ids[:, 21]], tbl_22[ids[:, 22]], tbl_23[ids[:, 23]], tbl_24[ids[:, 24]], tbl_25[ids[:, 25]]], axis=1)
    z = _L0_rec_ref(r_bottom_output, e)
    z = z.reshape(z.shape[0], -1)
    h = jnp.concatenate([z, r_bottom_output], axis=1)
    h = jnp.maximum(h @ W_top1 + b_top1, 0.0)
    h = jnp.maximum(h @ W_top2 + b_top2, 0.0)
    y = h @ W_top3
    return y

_drawn_inputs = setup_inputs


def setup_inputs(seed=0):
    import zlib

    import numpy as np

    out = dict(_drawn_inputs(seed))
    spreads = {'b_top1': (0.0, 0.1), 'b_top2': (0.0, 0.1)}
    factors = {}
    for name, (base, spread) in spreads.items():
        noise = np.random.default_rng([zlib.crc32(name.encode()), seed]).standard_normal(out[name].shape)
        drawn = base * np.exp(spread * noise) if base else spread * noise
        out[name] = jnp.asarray(drawn.astype(out[name].dtype))
    for name, factor in factors.items():
        out[name] = (out[name] * factor).astype(out[name].dtype)
    return out
```

```python
from contextlib import ExitStack

import concourse.bass as bass
from concourse import mybir

BATCH, DIM = 2048, 128
ROWS = [125000, 1250, 1000, 1250, 1250, 1000, 1250, 12500, 1000, 12500, 1000, 1250, 1000, 1000,
        12500, 1250, 1000, 12500, 1250, 1000, 12500, 1000, 1000, 1250, 12500, 1250]
ONEHOT = [2, 5, 8, 10, 12, 13]
GATHER = [t for t in range(26) if t not in ONEHOT]
N_OH, N_GA = len(ONEHOT), len(GATHER)
SLOTS = [0] + [t + 1 for t in ONEHOT] + [t + 1 for t in GATHER]
F = len(SLOTS)
FP = 32
P = 128
CHUNK = 256
CHUNKS = BATCH // CHUNK
TILES = CHUNK // P
BUFFERS = [(p, t) for p in range(2) for t in range(TILES)]
OH_ROWS = 1000
OH_P = 125
OH_K = OH_ROWS // OH_P
RING = OH_K
GROUP = 4
GROUPS = N_GA // GROUP
T_ITEMS = TILES * GROUPS
ITEMS = N_OH + T_ITEMS
PER_BANK = ITEMS // 2
T_PER_BANK = T_ITEMS // 2
SG = 4
PIECE = 8
PIECES = CHUNK // (SG * PIECE)
J = 7
KT = J + 1
H1, H2 = 512, 256
M1, M2 = H1 // P, H2 // P
BOTTOM = KT - 1

assert N_OH % 2 == 0 and N_GA % GROUP == 0 and ITEMS % 2 == 0


def program(nc, ids_g, ids_oh, bottom_t, tables, w1, b1, w2, b2, w3, out):
    f32, f32r, i32 = mybir.dt.float32, mybir.dt.float32r, mybir.dt.int32
    ALU, ACT = mybir.AluOpType, mybir.ActivationFunctionType

    with ExitStack() as ctx:
        def sb(name, shape, dt):
            return ctx.enter_context(nc.sbuf_tensor(name, shape, dt))

        def sem(name):
            return ctx.enter_context(nc.semaphore(name))

        idx_all = sb("idx_all", [P, CHUNKS * TILES + 1, N_GA], i32)
        idx = [[sb(f"idx{p}{t}", [P, N_GA], i32) for t in range(TILES)] for p in range(2)]
        E = [[sb(f"E{p}{t}", [P, N_GA, DIM], f32) for t in range(TILES)] for p in range(2)]
        ET = sb("ET", [P, CHUNK * FP], f32)
        Zf = sb("Zf", [P, KT, CHUNK], f32)
        Zhi = sb("Zhi", [P, KT, CHUNK], f32r)
        Zlo = sb("Zlo", [P, KT, CHUNK], f32r)
        W1hi = sb("W1hi", [P, KT * H1], f32r)
        W1lo = sb("W1lo", [P, KT * H1], f32r)
        Thi = sb("Thi", [OH_P, N_OH * OH_K * DIM], f32r)
        Tlo = sb("Tlo", [OH_P, N_OH * OH_K * DIM], f32r)
        onehot = [sb(f"onehot{k}", [OH_P, CHUNK], f32r) for k in range(RING)]
        ohid = sb("ohid", [OH_P, N_OH, CHUNK], i32)
        rowno_i = sb("rowno_i", [OH_P, OH_K], i32)
        rowno = sb("rowno", [OH_P, OH_K], f32)
        ident = sb("ident", [P, P], f32)
        W2 = sb("W2", [P, M1, H2], f32)
        W3 = sb("W3", [P, M2], f32)
        B1 = sb("B1", [P, M1], f32)
        B2 = sb("B2", [P, M2], f32)
        h1 = sb("h1", [P, M1, CHUNK], f32)
        h2 = sb("h2", [P, M2, CHUNK], f32)
        y = sb("y", [1, CHUNK], f32)

        def ps(name, shape):
            return ctx.enter_context(nc.psum_tensor(name, shape, f32))

        TB = [ps(f"TB{b}", [P, 512]) for b in range(2)]
        G = ps("G", [P, 4, 512])
        MB = [ps(f"MB{b}", [P, 512]) for b in range(2)]

        idx_loaded = sem("idx_loaded")
        idx_placed = sem("idx_placed")
        gathered = [[sem(f"gathered{p}{t}") for t in range(TILES)] for p in range(2)]
        tables_loaded = [sem(f"table_loaded{k}") for k in range(N_OH)]
        w1_loaded = sem("w1_loaded")
        small_loaded = sem("small_loaded")
        ohid_loaded = sem("ohid_loaded")
        bottom_loaded = sem("bottom_loaded")
        hi_split = sem("hi_split")
        lo_split = sem("lo_split")
        consts = sem("consts")
        set_up = sem("set_up")
        onehot_made = sem("onehot_made")
        onehot_used = sem("onehot_used")
        fill_full = [sem(f"fill_full{b}") for b in range(2)]
        fill_taken = [sem(f"fill_taken{b}") for b in range(2)]
        bottom_in_et = sem("bottom_in_et")
        gram_full = [sem(f"gram_full{h}") for h in range(2)]
        gram_taken = [sem(f"gram_taken{h}") for h in range(2)]
        zhi_done = sem("zhi_done")
        zlo_done = sem("zlo_done")
        m_full = [sem(f"m_full{b}") for b in range(2)]
        m_taken = [sem(f"m_taken{b}") for b in range(2)]
        y_stored = sem("y_stored")

        ETv = ET[:].rearrange("p (b f) -> p b f", f=FP)
        stage = ET
        TW = OH_K * DIM

        def t_slot(k):
            return slice(k * TW, (k + 1) * TW)

        def first(count):
            return isinstance(count, int) and count == 0

        def fill_item(m):
            return m % 2, m // 2

        def take_fill(eng, copy, c, m):
            b, n = fill_item(m)
            if m < N_OH:
                eng.wait_ge(onehot_used, (c * N_OH + m + 1) * OH_K)
                src, dst = TB[b][:, 0:CHUNK], ETv[:, :, 1 + m]
            else:
                t, g = divmod(m - N_OH, GROUPS)
                eng.wait_ge(fill_full[b], c * T_PER_BANK + (m - N_OH) // 2 + 1)
                src = TB[b][:].rearrange("p (f s) -> p s f", f=GROUP)
                f0 = 1 + N_OH + g * GROUP
                dst = ETv[:, t * P:(t + 1) * P, f0:f0 + GROUP]
            copy(dst, src).then_inc(fill_taken[b], 1)

        def take_gram(eng, copy, c, x):
            h = x % 2
            eng.wait_ge(gram_full[h], c * (PIECES // 2) + x // 2 + 1)
            v = G[:, 2 * h:2 * h + 2, :].rearrange("p b (n w) -> p (b n) w", w=P)
            for q in range(4):
                js = [j for j in range(J) if 0 < 4 * j + q < F]
                for s in range(SG):
                    src = v[32 * s:32 * s + F, :, s * F + 4 * js[0] + q:s * F + 4 * js[-1] + q + 1:4]
                    s0 = x * PIECE * SG + s
                    dst = Zf[32 * q:32 * q + F, js[0]:js[-1] + 1, s0:s0 + SG * (PIECE - 1) + 1:SG]
                    last = copy(dst, src.rearrange("p n j -> p j n"))
            last.then_inc(gram_taken[h], 1)

        block = ctx.enter_context(nc.Block())

        @block.sync
        def _(sp):
            sp.dma_start(idx_all[:, 0:CHUNKS * TILES, :],
                         ids_g.rearrange("(n p) f -> p n f", p=P)).then_inc(idx_loaded, 16)
            sp.dma_start(ohid[:], ids_oh[:, 0:CHUNK].partition_broadcast(OH_P)).then_inc(ohid_loaded, 16)
            for k in range(N_OH):
                sp.dma_start(stage[0:OH_P, t_slot(k)],
                             tables[ONEHOT[k]].rearrange("(p k) d -> p (k d)", k=OH_K))\
                    .then_inc(tables_loaded[k], 16)
            sp.dma_start(W2[:], w2).then_inc(small_loaded, 16)
            sp.dma_start(W3[:], w3).then_inc(small_loaded, 16)
            sp.dma_start(B1[:], b1).then_inc(small_loaded, 16)
            sp.dma_start(B2[:], b2).then_inc(small_loaded, 16)
            sp.wait_ge(set_up, 3)
            sp.dma_start(Zf[:, BOTTOM, :], bottom_t[:, 0:CHUNK]).then_inc(bottom_loaded, 16)
            sp.wait_ge(lo_split, N_OH)
            sp.dma_start(stage[:, 0:KT * H1], w1).then_inc(w1_loaded, 16)
            with sp.Fori(1, CHUNKS) as c:
                sp.wait_ge(onehot_made, c * (N_OH * OH_K))
                sp.dma_start(ohid[:], ids_oh[:, bass.ds(c * CHUNK, CHUNK)].partition_broadcast(OH_P))\
                    .then_inc(ohid_loaded, 16)
                sp.wait_ge(zhi_done, c)
                sp.wait_ge(zlo_done, c)
                sp.dma_start(Zf[:, BOTTOM, :], bottom_t[:, bass.ds(c * CHUNK, CHUNK)])\
                    .then_inc(bottom_loaded, 16)

        @block.gpsimd
        def _(pool):
            nc.gpsimd.iota(rowno_i[:], pattern=[[1, OH_K]], base=0, channel_multiplier=OH_K)\
                .then_inc(consts, 1)
            nc.gpsimd.memset(ident[:], 0.0).then_inc(consts, 1)
            nc.gpsimd.memset(idx_all[:, CHUNKS * TILES, :], 0).then_inc(consts, 1)
            pool.wait_ge(consts, 3)
            nc.gpsimd.affine_select(out=ident[:], in_=ident[:], compare_op=ALU.not_equal, fill=1.0,
                                    base=0, pattern=[[-1, P]], channel_multiplier=1).then_inc(consts, 1)

            def place(n, p, t):
                nc.gpsimd.tensor_copy(idx[p][t][:], idx_all[:, bass.ds(n, 1), :]
                                      .rearrange("p a f -> p (a f)")).then_inc(idx_placed, 1)

            def gather(n, p, t):
                for k, table in enumerate(GATHER):
                    pool.indirect_dma_start(
                        E[p][t][:, k, :], None, tables[table],
                        bass.IndirectOffsetOnAxis(ap=idx[p][t][:, k:k + 1], axis=0))\
                        .then_inc(gathered[p][t], 16)

            pool.wait_ge(idx_loaded, 16)
            for n, (p, t) in enumerate(BUFFERS):
                place(n, p, t)
            pool.wait_ge(idx_placed, len(BUFFERS))
            for n, (p, t) in enumerate(BUFFERS):
                gather(n, p, t)
            pool.wait_ge(gathered[0][0], 16 * N_GA)
            place(len(BUFFERS), 0, 0)
            with pool.Fori(1, CHUNKS // 2) as i:
                for k, (p, t) in enumerate(BUFFERS):
                    n = i * len(BUFFERS) + k
                    pool.wait_ge(idx_placed, n + 1)
                    m = N_OH + (t + 1) * GROUPS - 1
                    pool.wait_ge(fill_full[m % 2], i * (2 * T_PER_BANK)
                                 + ((m - N_OH) // 2 + 1 + (p - 2) * T_PER_BANK))
                    pn, tn = BUFFERS[(k + 1) % len(BUFFERS)]
                    pool.wait_ge(gathered[pn][tn], (i + (k + 1) // len(BUFFERS)) * (16 * N_GA))
                    place(n + 1, pn, tn)
                    gather(n, p, t)

        @block.tensor
        def _(pe):
            def fill_onehot(c):
                for k in range(N_OH):
                    b, n = fill_item(k)
                    if not first(c * PER_BANK + n):
                        pe.wait_ge(fill_taken[b], c * PER_BANK + n)
                    for kt in range(OH_K):
                        pe.wait_ge(onehot_made, (c * N_OH + k) * OH_K + (kt + 1))
                        w = slice(k * TW + kt * DIM, k * TW + (kt + 1) * DIM)
                        nc.tensor.matmul(TB[b][:, 0:CHUNK], Thi[:, w], onehot[kt][:],
                                         start=(kt == 0), stop=False)
                        nc.tensor.matmul(TB[b][:, 0:CHUNK], Tlo[:, w], onehot[kt][:],
                                         start=False, stop=(kt == OH_K - 1)).then_inc(onehot_used, 1)

            def fill_transposed(c, p, i, t):
                pe.wait_ge(gathered[p][t], (i + 1) * (16 * N_GA))
                for g in range(GROUPS):
                    b, n = fill_item(N_OH + t * GROUPS + g)
                    pe.wait_ge(fill_taken[b], c * PER_BANK + n)
                    for f in range(GROUP):
                        last = nc.tensor.transpose(TB[b][:, f * P:(f + 1) * P],
                                                   E[p][t][:, g * GROUP + f, :], ident[:])
                    last.then_inc(fill_full[b], 1)

            def gram(c):
                for b in range(2):
                    pe.wait_ge(fill_taken[b], (c + 1) * PER_BANK)
                pe.wait_ge(bottom_in_et, c + 1)
                for x in range(PIECES):
                    h = x % 2
                    if not first(c * (PIECES // 2) + x // 2):
                        pe.wait_ge(gram_taken[h], c * (PIECES // 2) + x // 2)
                    for n in range(PIECE):
                        s0 = (x * PIECE + n) * SG
                        last = nc.tensor.matmul(
                            G[:, 2 * h + n // 4, (n % 4) * P:(n % 4) * P + SG * F],
                            ET[:, s0 * FP:(s0 + SG) * FP], ETv[:, s0:s0 + SG, 0:F],
                            start=True, stop=True)
                    last.then_inc(gram_full[h], 1)

            def top1(c):
                pe.wait_ge(zlo_done, c + 1)
                for m in range(M1):
                    b = m % 2
                    if not first(c * (4 - b) + m // 2):
                        pe.wait_ge(m_taken[b], c * (4 - b) + m // 2)
                    o = MB[b][:, 0:CHUNK]
                    for k in range(KT):
                        w = slice(k * H1 + m * P, k * H1 + (m + 1) * P)
                        nc.tensor.matmul(o, W1hi[:, w], Zhi[:, k, :], start=(k == 0), stop=False)
                        nc.tensor.matmul(o, W1hi[:, w], Zlo[:, k, :], start=False, stop=False)
                        last = nc.tensor.matmul(o, W1lo[:, w], Zhi[:, k, :], start=False,
                                                stop=(k == KT - 1))
                    last.then_inc(m_full[b], 1)

            def top2(c):
                pe.wait_ge(m_taken[0], c * 4 + 2)
                pe.wait_ge(m_taken[1], c * 3 + 2)
                for m in range(M2):
                    for k in range(M1):
                        last = nc.tensor.matmul(MB[m][:, 0:CHUNK], W2[:, k, m * P:(m + 1) * P],
                                                h1[:, k, :], start=(k == 0), stop=(k == M1 - 1))
                    last.then_inc(m_full[m], 1)

            def top3(c):
                pe.wait_ge(m_taken[0], c * 4 + 3)
                pe.wait_ge(m_taken[1], c * 3 + 3)
                for k in range(M2):
                    last = nc.tensor.matmul(MB[0][0:1, 0:CHUNK], W3[:, k:k + 1], h2[:, k, :],
                                            start=(k == 0), stop=(k == M2 - 1))
                last.then_inc(m_full[0], 1)

            def step(c, p_next, i_next):
                gram(c)
                fill_onehot(c + 1)
                top1(c)
                fill_transposed(c + 1, p_next, i_next, 0)
                top2(c)
                fill_transposed(c + 1, p_next, i_next, 1)
                top3(c)

            pe.wait_ge(consts, 4)
            pe.wait_ge(lo_split, N_OH + 1)
            pe.wait_ge(small_loaded, 4 * 16)
            fill_onehot(0)
            for t in range(TILES):
                fill_transposed(0, 0, 0, t)
            step(0, 1, 0)
            with pe.Fori(0, CHUNKS // 2 - 1) as i:
                step(i * 2 + 1, 0, i + 1)
                step(i * 2 + 2, 1, i + 1)
            gram(CHUNKS - 1)
            top1(CHUNKS - 1)
            top2(CHUNKS - 1)
            top3(CHUNKS - 1)

        @block.vector
        def _(dve):
            def copy(dst, src):
                return nc.vector.tensor_copy(dst, src)

            def make_onehot(c, k):
                for kt in range(OH_K):
                    if not first((c * N_OH + k) * OH_K):
                        dve.wait_ge(onehot_used, (c * N_OH + (k - 1)) * OH_K + (kt + 1))
                    nc.vector.tensor_single_scalar(onehot[kt][:], ohid[:, k, :], rowno[:, kt:kt + 1],
                                                   ALU.is_equal).then_inc(onehot_made, 1)

            def lo_part(lo, full, hi):
                return nc.vector.tensor_tensor(lo, full, hi.bitcast(f32), ALU.subtract)

            def first_onehot(c):
                dve.wait_ge(ohid_loaded, (c + 1) * 16)
                make_onehot(c, 0)

            def fill_onehot(c):
                for k in range(N_OH):
                    if k + 1 < N_OH:
                        make_onehot(c, k + 1)
                    if k % 2 == 0:
                        take_fill(dve, copy, c, k)

            def fill_transposed(c, t):
                for m in range(N_OH + t * GROUPS, N_OH + (t + 1) * GROUPS):
                    if m % 2 == 0:
                        take_fill(dve, copy, c, m)

            def take_layer(c, n, dst, bias):
                dve.wait_ge(m_full[1], c * 3 + (n + 1))
                nc.vector.tensor_scalar(dst, MB[1][:, 0:CHUNK], bias, 0.0, ALU.add, ALU.max)\
                    .then_inc(m_taken[1], 1)

            def gram(c):
                if not first(c):
                    dve.wait_ge(zhi_done, c)
                    dve.wait_ge(zlo_done, c)
                for x in range(0, PIECES, 2):
                    take_gram(dve, copy, c, x)
                dve.wait_ge(zhi_done, c + 1)
                lo_part(Zlo[:], Zf[:], Zhi[:]).then_inc(zlo_done, 1)

            def step(c):
                first_onehot(c + 1)
                gram(c)
                fill_onehot(c + 1)
                for m in (1, 3):
                    take_layer(c, m // 2, h1[:, m, :], B1[:, m:m + 1])
                fill_transposed(c + 1, 0)
                take_layer(c, 2, h2[:, 1, :], B2[:, 1:2])
                fill_transposed(c + 1, 1)

            dve.wait_ge(consts, 4)
            nc.vector.tensor_copy(rowno[:], rowno_i[:]).then_inc(set_up, 1)
            nc.vector.memset(y[:], 0.0).then_inc(set_up, 1)
            nc.vector.memset(Zf[:], 0.0).then_inc(set_up, 1)
            dve.wait_ge(set_up, 3)
            for k in range(N_OH):
                dve.wait_ge(hi_split, k + 1)
                lo_part(Tlo[:, t_slot(k)], stage[0:OH_P, t_slot(k)], Thi[:, t_slot(k)])\
                    .then_inc(lo_split, 1)
            first_onehot(0)
            dve.wait_ge(hi_split, N_OH + 1)
            lo_part(W1lo[:], stage[:, 0:KT * H1], W1hi[:]).then_inc(lo_split, 1)
            dve.wait_ge(lo_split, N_OH + 1)
            nc.vector.memset(ETv[:, :, F:FP], 0.0).then_inc(set_up, 1)
            dve.wait_ge(small_loaded, 4 * 16)
            fill_onehot(0)
            for t in range(TILES):
                fill_transposed(0, t)
            step(0)
            with dve.Fori(1, CHUNKS - 1) as c:
                step(c)
            c = CHUNKS - 1
            gram(c)
            for m in (1, 3):
                take_layer(c, m // 2, h1[:, m, :], B1[:, m:m + 1])
            take_layer(c, 2, h2[:, 1, :], B2[:, 1:2])

        @block.scalar
        def _(act):
            def copy(dst, src):
                return nc.scalar.activation(dst, src, ACT.Copy)

            def fill_onehot(c):
                for k in range(1, N_OH, 2):
                    take_fill(act, copy, c, k)
                act.wait_ge(bottom_loaded, (c + 1) * 16)
                copy(ETv[:, :, 0], Zf[:, BOTTOM, :]).then_inc(bottom_in_et, 1)

            def fill_transposed(c, t):
                for m in range(N_OH + t * GROUPS, N_OH + (t + 1) * GROUPS):
                    if m % 2:
                        take_fill(act, copy, c, m)

            def take_layer(c, n, dst, bias):
                act.wait_ge(m_full[0], c * 4 + (n + 1))
                nc.scalar.activation(dst, MB[0][:, 0:CHUNK], ACT.Relu, bias=bias)\
                    .then_inc(m_taken[0], 1)

            def gram(c):
                if not first(c):
                    act.wait_ge(zlo_done, c)
                    act.wait_ge(zhi_done, c)
                for x in range(1, PIECES, 2):
                    take_gram(act, copy, c, x)
                for h in range(2):
                    act.wait_ge(gram_taken[h], (c + 1) * (PIECES // 2))
                act.wait_ge(bottom_loaded, (c + 1) * 16)
                copy(Zhi[:], Zf[:]).then_inc(zhi_done, 1)

            def take_y(c):
                act.wait_ge(m_full[0], c * 4 + 4)
                if not first(c):
                    act.wait_ge(y_stored, c * 16)
                copy(y[:], MB[0][0:1, 0:CHUNK]).then_inc(m_taken[0], 1)
                act.wait_ge(m_taken[0], c * 4 + 4)
                act.dma_start(out[:, bass.ds(c * CHUNK, CHUNK)], y[:]).then_inc(y_stored, 16)

            def step(c):
                gram(c)
                fill_onehot(c + 1)
                for m in (0, 2):
                    take_layer(c, m // 2, h1[:, m, :], B1[:, m:m + 1])
                fill_transposed(c + 1, 0)
                take_layer(c, 2, h2[:, 0, :], B2[:, 0:1])
                fill_transposed(c + 1, 1)
                take_y(c)

            for k in range(N_OH):
                act.wait_ge(tables_loaded[k], 16)
                copy(Thi[:, t_slot(k)], stage[0:OH_P, t_slot(k)]).then_inc(hi_split, 1)
            act.wait_ge(w1_loaded, 16)
            copy(W1hi[:], stage[:, 0:KT * H1]).then_inc(hi_split, 1)
            act.wait_ge(small_loaded, 4 * 16)
            act.wait_ge(set_up, 4)
            fill_onehot(0)
            for t in range(TILES):
                fill_transposed(0, t)
            step(0)
            with act.Fori(1, CHUNKS - 1) as c:
                step(c)
            c = CHUNKS - 1
            gram(c)
            for m in (0, 2):
                take_layer(c, m // 2, h1[:, m, :], B1[:, m:m + 1])
            take_layer(c, 2, h2[:, 0, :], B2[:, 0:1])
            take_y(c)
            act.wait_ge(y_stored, CHUNKS * 16)


def pair_rows():
    import numpy as np
    slot = {feature: n for n, feature in enumerate(SLOTS)}
    at = []
    for i, j in zip(*np.triu_indices(F, k=1)):
        a, b = sorted((slot[int(i)], slot[int(j)]))
        at.append((b % 4, a, b // 4))
    return np.array(at).T


def kernel(**inputs):
    import numpy as np
    import concourse.bacc as bacc
    from concourse import mybir as mb
    from concourse.bass_utils import run_bass_kernel_spmd

    x = {k: np.asarray(v) for k, v in inputs.items()}
    w1 = x["W_top1"]
    w1_laid = np.zeros((4, 32, KT, H1), w1.dtype)
    q, a, j = pair_rows()
    w1_laid[q, a, j] = w1[:len(q)]
    w1_laid.reshape(P, KT, H1)[:, BOTTOM] = w1[len(q):]
    laid = {
        "ids_g": x["ids"][:, GATHER],
        "ids_oh": x["ids"].T[ONEHOT],
        "bottom_t": x["r_bottom_output"].T,
        "w1": w1_laid.reshape(P, KT * H1),
        "b1": x["b_top1"].reshape(M1, P).T,
        "w2": x["W_top2"].reshape(M1, P, H2).transpose(1, 0, 2),
        "b2": x["b_top2"].reshape(M2, P).T,
        "w3": x["W_top3"].reshape(M2, P).T,
    }
    for t in range(26):
        laid[f"tbl_{t}"] = x[f"tbl_{t}"]
    nc = bacc.Bacc("TRN2", target_bir_lowering=False, num_devices=1)
    arrays, aps = {}, {}
    for name, v in laid.items():
        v = np.ascontiguousarray(v)
        arrays[f"in_{name}"] = v
        aps[name] = nc.dram_tensor(f"in_{name}", v.shape, mb.dt.from_np(v.dtype), kind="ExternalInput").ap()
    out = nc.dram_tensor("out_y", (1, BATCH), mb.dt.float32, kind="ExternalOutput").ap()
    tables = [aps.pop(f"tbl_{t}") for t in range(26)]
    program(nc, tables=tables, out=out, **aps)
    r = run_bass_kernel_spmd(nc, [arrays], core_ids=[0])
    return r.results[0]["out_y"].reshape(BATCH, 1)
```

```python
from contextlib import ExitStack

import concourse.bass as bass
from concourse import mybir

BATCH, DIM = 2048, 128
ROWS = [125000, 1250, 1000, 1250, 1250, 1000, 1250, 12500, 1000, 12500, 1000, 1250, 1000, 1000,
        12500, 1250, 1000, 12500, 1250, 1000, 12500, 1000, 1000, 1250, 12500, 1250]
ONEHOT = [2, 5, 8, 10, 12, 13]
GATHER = [t for t in range(26) if t not in ONEHOT]
N_OH, N_GA = len(ONEHOT), len(GATHER)
SLOTS = [0] + [t + 1 for t in ONEHOT] + [t + 1 for t in GATHER]
F = len(SLOTS)
FP = 32
P = 128
CHUNK = 256
CHUNKS = BATCH // CHUNK
TILES = CHUNK // P
BUFFERS = [(p, t) for p in range(2) for t in range(TILES)]
OH_ROWS = 1000
OH_P = 125
OH_K = OH_ROWS // OH_P
RING = OH_K
GROUP = 4
GROUPS = N_GA // GROUP
T_ITEMS = TILES * GROUPS
BANK = [m % 2 for m in range(N_OH)] + [(2, 3, 0, 1)[m % 4] for m in range(T_ITEMS)]
PLACE = [BANK[:m].count(b) for m, b in enumerate(BANK)]
PER_BANK = [BANK.count(b) for b in range(4)]
TAKER = ["act"] * N_OH + [("dve", "act")[m % 2] for m in range(T_ITEMS)]
SG = 4
A = F - 1
GROWS = (SG - 1) * FP + A
PIECE = 8
PIECES = CHUNK // (SG * PIECE)
SAMPLES = {"dve": (0, 1), "act": (2, 3)}
PART = 64
PARTS = CHUNK // PART
J = 7
KT = J + 1
H1, H2 = 512, 256
M1, M2 = H1 // P, H2 // P
BOTTOM = KT - 1

assert N_OH == 6 and N_GA % GROUP == 0


def program(nc, ids_g, ids_oh, bottom_t, tables, w1, b1, w2, b2, w3, out):
    f32, f32r, i32 = mybir.dt.float32, mybir.dt.float32r, mybir.dt.int32
    ALU, ACT = mybir.AluOpType, mybir.ActivationFunctionType

    with ExitStack() as ctx:
        def sb(name, shape, dt):
            return ctx.enter_context(nc.sbuf_tensor(name, shape, dt))

        def sem(name):
            return ctx.enter_context(nc.semaphore(name))

        idx_all = sb("idx_all", [P, CHUNKS * TILES + 1, N_GA], i32)
        idx = [[sb(f"idx{p}{t}", [P, N_GA], i32) for t in range(TILES)] for p in range(2)]
        E = [[sb(f"E{p}{t}", [P, N_GA, DIM], f32) for t in range(TILES)] for p in range(2)]
        ET = sb("ET", [P, CHUNK * FP], f32)
        Zf = sb("Zf", [P, KT, CHUNK], f32)
        Zhi = sb("Zhi", [P, KT, CHUNK], f32r)
        Zlo = sb("Zlo", [P, KT, CHUNK], f32r)
        W1hi = sb("W1hi", [P, KT * H1], f32r)
        W1lo = sb("W1lo", [P, KT * H1], f32r)
        Thi = sb("Thi", [OH_P, N_OH * OH_K * DIM], f32r)
        Tlo = sb("Tlo", [OH_P, N_OH * OH_K * DIM], f32r)
        onehot = [sb(f"onehot{k}", [OH_P, CHUNK], f32r) for k in range(RING)]
        ohid = sb("ohid", [OH_P, N_OH, CHUNK], i32)
        row0_i = sb("row0_i", [OH_P, 1], i32)
        row0 = sb("row0", [OH_P, 1], f32)
        ident = sb("ident", [P, P], f32)
        W2 = sb("W2", [P, M1, H2], f32)
        W3 = sb("W3", [P, M2], f32)
        B1 = sb("B1", [P, M1], f32)
        B2 = sb("B2", [P, M2], f32)
        h1 = sb("h1", [P, M1, CHUNK], f32)
        h2 = sb("h2", [P, M2, CHUNK], f32)
        h2w = sb("h2w", [P, CHUNK], f32)
        ones = sb("ones", [P, 1], f32)
        y = sb("y", [1, CHUNK], f32)

        def ps(name, shape):
            return ctx.enter_context(nc.psum_tensor(name, shape, f32))

        G = ps("G", [P, 4, 512])
        FB = [ps("FB0", [P, 512])[:], ps("FB1", [P, 512])[:], G[:, 0, :], G[:, 2, :]]
        MB = [ps(f"MB{b}", [P, 512]) for b in range(2)]

        idx_loaded = sem("idx_loaded")
        idx_placed = sem("idx_placed")
        gathered = [[sem(f"gathered{p}{t}") for t in range(TILES)] for p in range(2)]
        tables_loaded = [sem(f"table_loaded{k}") for k in range(N_OH)]
        w1_loaded = [sem(f"w1_loaded{n}") for n in range(2)]
        small_loaded = sem("small_loaded")
        ohid_loaded = sem("ohid_loaded")
        ohid_shifted = sem("ohid_shifted")
        bottom_loaded = sem("bottom_loaded")
        hi_split = sem("hi_split")
        lo_split = sem("lo_split")
        consts = sem("consts")
        set_up = sem("set_up")
        onehot_made = sem("onehot_made")
        onehot_used = sem("onehot_used")
        transposed = sem("transposed")
        fill_taken = [sem(f"fill_taken{b}") for b in range(4)]
        bottom_in_et = sem("bottom_in_et")
        gram_full = sem("gram_full")
        gram_taken = {e: sem(f"gram_taken_{e}") for e in SAMPLES}
        zhi_done = sem("zhi_done")
        zlo_done = sem("zlo_done")
        m_full = [sem(f"m_full{b}") for b in range(2)]
        m_taken = [sem(f"m_taken{b}") for b in range(2)]
        half_weighted = sem("half_weighted")
        weighted = sem("weighted")
        y_stored = sem("y_stored")

        ETv = ET[:].rearrange("p (b f) -> p b f", f=FP)
        Ev = [E[1][t][:].rearrange("p f d -> p (f d)") for t in range(TILES)]
        TW = OH_K * DIM

        HW = KT * H1 // 2

        def t_slot(k):
            return slice(k * TW, (k + 1) * TW)

        stage = [v[0:OH_P, t_slot(k)] for v in (Ev[0], Ev[1], Zf[:].rearrange("p k b -> p (k b)"))
                 for k in range(2)] + [v[:, 0:HW] for v in Ev]
        hi_of = [Thi[:, t_slot(k)] for k in range(N_OH)] + [W1hi[:, n * HW:(n + 1) * HW] for n in range(2)]
        lo_of = [Tlo[:, t_slot(k)] for k in range(N_OH)] + [W1lo[:, n * HW:(n + 1) * HW] for n in range(2)]

        def first(count):
            return isinstance(count, int) and count <= 0

        def last_item(t):
            return N_OH + (t + 1) * GROUPS - 1

        def take_fill(who, eng, copy, c, m):
            if TAKER[m] != who:
                return
            if m < N_OH:
                eng.wait_ge(onehot_used, (c * N_OH + m + 1) * OH_K)
                src, dst = FB[BANK[m]][:, 0:CHUNK], ETv[:, :, 1 + m]
            else:
                t, g = divmod(m - N_OH, GROUPS)
                eng.wait_ge(transposed, c * T_ITEMS + (m - N_OH + 1))
                src = FB[BANK[m]].rearrange("p (f s) -> p s f", f=GROUP)
                f0 = 1 + N_OH + g * GROUP
                dst = ETv[:, t * P:(t + 1) * P, f0:f0 + GROUP]
            copy(dst, src).then_inc(fill_taken[BANK[m]], 1)

        def take_gram(who, eng, copy, c, x):
            h = x % 2
            eng.wait_ge(gram_full, c * PIECES + (x + 1))
            v = G[:, 2 * h:2 * h + 2, :].rearrange("p b (n w) -> p (b n) w", w=P)
            for q in range(4):
                js = [j for j in range(J) if 0 < 4 * j + q < F]
                b0, b1 = 4 * js[0] + q - 1, 4 * js[-1] + q - 1
                for s in SAMPLES[who]:
                    src = v[FP * s:FP * s + A, :, s * A + b0:s * A + b1 + 1:4]
                    s0 = x * PIECE * SG + s
                    dst = Zf[FP * q:FP * q + A, js[0]:js[-1] + 1, s0:s0 + SG * (PIECE - 1) + 1:SG]
                    last = copy(dst, src.rearrange("p n j -> p j n"))
            last.then_inc(gram_taken[who], 1)

        block = ctx.enter_context(nc.Block())

        @block.sync
        def _(sp):
            sp.dma_start(idx_all[:, 0:CHUNKS * TILES, :],
                         ids_g.rearrange("(n p) f -> p n f", p=P)).then_inc(idx_loaded, 16)
            sp.dma_start(ohid[:], ids_oh[:, 0:CHUNK].partition_broadcast(OH_P)).then_inc(ohid_loaded, 16)
            for k in range(N_OH):
                sp.dma_start(stage[k], tables[ONEHOT[k]].rearrange("(p k) d -> p (k d)", k=OH_K))\
                    .then_inc(tables_loaded[k], 16)
            sp.dma_start(W2[:], w2).then_inc(small_loaded, 16)
            sp.dma_start(W3[:], w3).then_inc(small_loaded, 16)
            sp.dma_start(B1[:], b1).then_inc(small_loaded, 16)
            sp.dma_start(B2[:], b2).then_inc(small_loaded, 16)
            for n in range(2):
                sp.wait_ge(lo_split, 2 * (n + 1))
                sp.dma_start(stage[N_OH + n], w1[:, n * HW:(n + 1) * HW]).then_inc(w1_loaded[n], 16)
            sp.wait_ge(set_up, 4)
            sp.dma_start(Zf[:, BOTTOM, :], bottom_t[:, 0:CHUNK]).then_inc(bottom_loaded, 16)
            with sp.Fori(1, CHUNKS) as c:
                sp.wait_ge(onehot_made, c * (N_OH * OH_K))
                sp.dma_start(ohid[:], ids_oh[:, bass.ds(c * CHUNK, CHUNK)].partition_broadcast(OH_P))\
                    .then_inc(ohid_loaded, 16)
                sp.wait_ge(zhi_done, c * PARTS)
                sp.wait_ge(zlo_done, c * PARTS)
                sp.dma_start(Zf[:, BOTTOM, :], bottom_t[:, bass.ds(c * CHUNK, CHUNK)])\
                    .then_inc(bottom_loaded, 16)

        @block.gpsimd
        def _(pool):
            nc.gpsimd.iota(row0_i[:], pattern=[[0, 1]], base=0, channel_multiplier=OH_K)\
                .then_inc(consts, 1)
            nc.gpsimd.memset(ident[:], 0.0).then_inc(consts, 1)
            nc.gpsimd.memset(idx_all[:, CHUNKS * TILES, :], 0).then_inc(consts, 1)
            pool.wait_ge(consts, 3)
            nc.gpsimd.affine_select(out=ident[:], in_=ident[:], compare_op=ALU.not_equal, fill=1.0,
                                    base=0, pattern=[[-1, P]], channel_multiplier=1).then_inc(consts, 1)

            def place(n, p, t):
                nc.gpsimd.tensor_copy(idx[p][t][:], idx_all[:, bass.ds(n, 1), :]
                                      .rearrange("p a f -> p (a f)")).then_inc(idx_placed, 1)

            def gather(n, p, t):
                for k, table in enumerate(GATHER):
                    pool.indirect_dma_start(
                        E[p][t][:, k, :], None, tables[table],
                        bass.IndirectOffsetOnAxis(ap=idx[p][t][:, k:k + 1], axis=0))\
                        .then_inc(gathered[p][t], 16)

            pool.wait_ge(idx_loaded, 16)
            for n, (p, t) in enumerate(BUFFERS):
                place(n, p, t)
            pool.wait_ge(idx_placed, len(BUFFERS))
            for n, (p, t) in enumerate(BUFFERS):
                if p:
                    pool.wait_ge(lo_split, N_OH + 2)
                gather(n, p, t)
            pool.wait_ge(gathered[0][0], 16 * N_GA)
            place(len(BUFFERS), 0, 0)
            with pool.Fori(1, CHUNKS // 2) as i:
                for k, (p, t) in enumerate(BUFFERS):
                    n = i * len(BUFFERS) + k
                    pool.wait_ge(idx_placed, n + 1)
                    pool.wait_ge(transposed, i * (2 * T_ITEMS) + ((p - 2) * T_ITEMS + (t + 1) * GROUPS))
                    pn, tn = BUFFERS[(k + 1) % len(BUFFERS)]
                    pool.wait_ge(gathered[pn][tn], (i + (k + 1) // len(BUFFERS)) * (16 * N_GA))
                    place(n + 1, pn, tn)
                    gather(n, p, t)

        @block.tensor
        def _(pe):
            def free_bank(c, m):
                if not first(c * PER_BANK[BANK[m]] + PLACE[m]):
                    pe.wait_ge(fill_taken[BANK[m]], c * PER_BANK[BANK[m]] + PLACE[m])

            def fill_onehot(c):
                for k in range(N_OH):
                    o = FB[BANK[k]][:, 0:CHUNK]
                    free_bank(c, k)
                    if first(c):
                        pe.wait_ge(lo_split, k + 1)
                    for kt in range(OH_K):
                        pe.wait_ge(onehot_made, (c * N_OH + k) * OH_K + (kt + 1))
                        w = slice(k * TW + kt * DIM, k * TW + (kt + 1) * DIM)
                        nc.tensor.matmul(o, Thi[:, w], onehot[kt][:], start=(kt == 0), stop=False)
                        nc.tensor.matmul(o, Tlo[:, w], onehot[kt][:], start=False,
                                         stop=(kt == OH_K - 1)).then_inc(onehot_used, 1)

            def fill_transposed(c, p, i, t):
                pe.wait_ge(gathered[p][t], (i + 1) * (16 * N_GA))
                for g in range(GROUPS):
                    m = N_OH + t * GROUPS + g
                    free_bank(c, m)
                    for f in range(GROUP):
                        last = nc.tensor.transpose(FB[BANK[m]][:, f * P:(f + 1) * P],
                                                   E[p][t][:, g * GROUP + f, :], ident[:])
                    last.then_inc(transposed, 1)

            def gram(c, t, filled=TILES - 1):
                pe.wait_ge(bottom_in_et, c + 1)
                for b in range(4):
                    pe.wait_ge(fill_taken[b], c * PER_BANK[b] + BANK[:last_item(filled) + 1].count(b))
                for x in range(t * PIECES // TILES, (t + 1) * PIECES // TILES):
                    h = x % 2
                    if not first(c * PIECES + (x - 1)):
                        pe.wait_ge(gram_taken["dve"], c * PIECES + (x - 1))
                        pe.wait_ge(gram_taken["act"], c * PIECES + (x - 1))
                    for n in range(PIECE):
                        s0 = (x * PIECE + n) * SG
                        last = nc.tensor.matmul(
                            G[0:GROWS, 2 * h + n // 4, (n % 4) * P:(n % 4) * P + SG * A],
                            ET[:, s0 * FP:s0 * FP + GROWS], ETv[:, s0:s0 + SG, 1:F],
                            start=True, stop=True)
                    last.then_inc(gram_full, 1)

            def top1(c):
                pe.wait_ge(zlo_done, (c + 1) * PARTS)
                for m in range(M1):
                    b = m % 2
                    if not first(c * (4 - b) + m // 2):
                        pe.wait_ge(m_taken[b], c * (4 - b) + m // 2)
                    o = MB[b][:, 0:CHUNK]
                    for k in range(KT):
                        w = slice(k * H1 + m * P, k * H1 + (m + 1) * P)
                        nc.tensor.matmul(o, W1hi[:, w], Zhi[:, k, :], start=(k == 0), stop=False)
                        nc.tensor.matmul(o, W1hi[:, w], Zlo[:, k, :], start=False, stop=False)
                        last = nc.tensor.matmul(o, W1lo[:, w], Zhi[:, k, :], start=False,
                                                stop=(k == KT - 1))
                    last.then_inc(m_full[b], 1)

            def top2(c):
                pe.wait_ge(m_taken[0], c * 4 + 2)
                pe.wait_ge(m_taken[1], c * 3 + 2)
                for m in range(M2):
                    for k in range(M1):
                        last = nc.tensor.matmul(MB[m][:, 0:CHUNK], W2[:, k, m * P:(m + 1) * P],
                                                h1[:, k, :], start=(k == 0), stop=(k == M1 - 1))
                    last.then_inc(m_full[m], 1)

            def top3(c):
                pe.wait_ge(weighted, c + 1)
                nc.tensor.matmul(MB[0][0:1, 0:CHUNK], ones[:], h2w[:], start=True, stop=True)\
                    .then_inc(m_full[0], 1)

            def step(c, p_next, i_next):
                gram(c, 0)
                gram(c, 1)
                rest_of_step(c, p_next, i_next)

            def rest_of_step(c, p_next, i_next):
                fill_onehot(c + 1)
                top1(c)
                fill_transposed(c + 1, p_next, i_next, 0)
                top2(c)
                fill_transposed(c + 1, p_next, i_next, 1)
                top3(c)

            pe.wait_ge(consts, 4)
            fill_onehot(0)
            fill_transposed(0, 0, 0, 0)
            gram(0, 0, filled=0)
            pe.wait_ge(gram_taken["dve"], PIECES // TILES)
            pe.wait_ge(gram_taken["act"], PIECES // TILES)
            fill_transposed(0, 0, 0, 1)
            gram(0, 1)
            pe.wait_ge(lo_split, N_OH + 2)
            pe.wait_ge(small_loaded, 4 * 16)
            rest_of_step(0, 1, 0)
            with pe.Fori(0, CHUNKS // 2 - 1) as i:
                step(i * 2 + 1, 0, i + 1)
                step(i * 2 + 2, 1, i + 1)
            c = CHUNKS - 1
            gram(c, 0)
            gram(c, 1)
            top1(c)
            top2(c)
            top3(c)

        @block.vector
        def _(dve):
            def copy(dst, src):
                return nc.vector.tensor_copy(dst, src)

            def make_onehot(c, k):
                for kt in range(OH_K):
                    if not first((c * N_OH + k) * OH_K):
                        dve.wait_ge(onehot_used, (c * N_OH + (k - 1)) * OH_K + (kt + 1))
                    nc.vector.tensor_single_scalar(onehot[kt][:], ohid[:, k, :].bitcast(f32), float(kt),
                                                   ALU.is_equal).then_inc(onehot_made, 1)

            def lo_part(lo, full, hi):
                return nc.vector.tensor_tensor(lo, full, hi.bitcast(f32), ALU.subtract)

            def first_onehot(c):
                dve.wait_ge(ohid_loaded, (c + 1) * 16)
                nc.vector.tensor_scalar(ohid[:].bitcast(f32), ohid[:], row0[:], None, ALU.subtract)\
                    .then_inc(ohid_shifted, 1)
                dve.wait_ge(ohid_shifted, c + 1)
                make_onehot(c, 0)

            def fill_transposed(c, t):
                for m in range(N_OH + t * GROUPS, N_OH + (t + 1) * GROUPS):
                    take_fill("dve", dve, copy, c, m)

            def take_layer(c, n, dst, bias):
                dve.wait_ge(m_full[1], c * 3 + (n + 1))
                nc.vector.tensor_scalar(dst, MB[1][:, 0:CHUNK], bias, 0.0, ALU.add, ALU.max)\
                    .then_inc(m_taken[1], 1)

            def weigh(c):
                dve.wait_ge(m_taken[0], c * 4 + 3)
                nc.vector.tensor_scalar(h2w[:], h2[:, 0, :], W3[:, 0:1], None, ALU.mult)\
                    .then_inc(half_weighted, 1)
                dve.wait_ge(m_taken[1], c * 3 + 3)
                dve.wait_ge(half_weighted, c + 1)
                nc.vector.scalar_tensor_tensor(h2w[:], h2[:, 1, :], W3[:, 1:2], h2w[:],
                                               ALU.mult, ALU.add).then_inc(weighted, 1)

            def cut_lo(c, r):
                at = slice(r * PART, (r + 1) * PART)
                dve.wait_ge(zhi_done, c * PARTS + (r + 1))
                lo_part(Zlo[:, :, at], Zf[:, :, at], Zhi[:, :, at]).then_inc(zlo_done, 1)

            def gram(c, t):
                if t == 0 and not first(c):
                    dve.wait_ge(zhi_done, c * PARTS)
                    dve.wait_ge(zlo_done, c * PARTS)
                for x in range(t * PIECES // TILES, (t + 1) * PIECES // TILES):
                    take_gram("dve", dve, copy, c, x)
                    if x % 2 == 0 and x:
                        cut_lo(c, x // 2 - 1)

            def rest_of_step(c):
                make_onehot(c + 1, 1)
                cut_lo(c, PARTS - 1)
                for k in range(2, N_OH):
                    make_onehot(c + 1, k)
                for m in (1, 3):
                    take_layer(c, m // 2, h1[:, m, :], B1[:, m:m + 1])
                fill_transposed(c + 1, 0)
                take_layer(c, 2, h2[:, 1, :], B2[:, 1:2])
                weigh(c)
                fill_transposed(c + 1, 1)

            def step(c):
                first_onehot(c + 1)
                gram(c, 0)
                gram(c, 1)
                rest_of_step(c)

            dve.wait_ge(consts, 4)
            nc.vector.tensor_copy(row0[:], row0_i[:]).then_inc(set_up, 1)
            nc.vector.memset(ones[:], 1.0).then_inc(set_up, 1)
            nc.vector.memset(ETv[:, :, F:FP], 0.0).then_inc(set_up, 1)
            dve.wait_ge(set_up, 3)
            first_onehot(0)
            for k in range(N_OH):
                dve.wait_ge(hi_split, k + 1)
                lo_part(lo_of[k], stage[k], hi_of[k]).then_inc(lo_split, 1)
                if k:
                    make_onehot(0, k)
            fill_transposed(0, 0)
            dve.wait_ge(set_up, 4)
            gram(0, 0)
            for k in (N_OH, N_OH + 1):
                dve.wait_ge(hi_split, k + 1)
                lo_part(lo_of[k], stage[k], hi_of[k]).then_inc(lo_split, 1)
            first_onehot(1)
            fill_transposed(0, 1)
            gram(0, 1)
            dve.wait_ge(small_loaded, 4 * 16)
            rest_of_step(0)
            with dve.Fori(1, CHUNKS - 1) as c:
                step(c)
            c = CHUNKS - 1
            gram(c, 0)
            gram(c, 1)
            cut_lo(c, PARTS - 1)
            for m in (1, 3):
                take_layer(c, m // 2, h1[:, m, :], B1[:, m:m + 1])
            take_layer(c, 2, h2[:, 1, :], B2[:, 1:2])
            weigh(c)

        @block.scalar
        def _(act):
            def copy(dst, src):
                return nc.scalar.activation(dst, src, ACT.Copy)

            def fill_onehot(c):
                for k in range(N_OH):
                    take_fill("act", act, copy, c, k)
                act.wait_ge(bottom_loaded, (c + 1) * 16)
                copy(ETv[:, :, 0], Zf[:, BOTTOM, :]).then_inc(bottom_in_et, 1)

            def fill_transposed(c, t):
                for m in range(N_OH + t * GROUPS, N_OH + (t + 1) * GROUPS):
                    take_fill("act", act, copy, c, m)

            def take_layer(c, n, dst, bias):
                act.wait_ge(m_full[0], c * 4 + (n + 1))
                nc.scalar.activation(dst, MB[0][:, 0:CHUNK], ACT.Relu, bias=bias)\
                    .then_inc(m_taken[0], 1)

            def gram(c, t):
                if t == 0 and not first(c):
                    act.wait_ge(zlo_done, c * PARTS)
                    act.wait_ge(zhi_done, c * PARTS)
                for x in range(t * PIECES // TILES, (t + 1) * PIECES // TILES):
                    take_gram("act", act, copy, c, x)
                    if x % 2:
                        for who in SAMPLES:
                            act.wait_ge(gram_taken[who], c * PIECES + (x + 1))
                        at = slice(x // 2 * PART, (x // 2 + 1) * PART)
                        copy(Zhi[:, :, at], Zf[:, :, at]).then_inc(zhi_done, 1)

            def take_y(c):
                act.wait_ge(m_full[0], c * 4 + 4)
                if not first(c):
                    act.wait_ge(y_stored, c * 16)
                copy(y[:], MB[0][0:1, 0:CHUNK]).then_inc(m_taken[0], 1)
                act.wait_ge(m_taken[0], c * 4 + 4)
                act.dma_start(out[:, bass.ds(c * CHUNK, CHUNK)], y[:]).then_inc(y_stored, 16)

            def rest_of_step(c):
                fill_onehot(c + 1)
                for m in (0, 2):
                    take_layer(c, m // 2, h1[:, m, :], B1[:, m:m + 1])
                fill_transposed(c + 1, 0)
                take_layer(c, 2, h2[:, 0, :], B2[:, 0:1])
                fill_transposed(c + 1, 1)
                take_y(c)

            def step(c):
                gram(c, 0)
                gram(c, 1)
                rest_of_step(c)

            act.wait_ge(set_up, 3)
            for k in range(N_OH):
                act.wait_ge(tables_loaded[k], 16)
                copy(hi_of[k], stage[k]).then_inc(hi_split, 1)
                if k:
                    take_fill("act", act, copy, 0, k - 1)
            take_fill("act", act, copy, 0, N_OH - 1)
            act.wait_ge(lo_split, N_OH)
            nc.scalar.memzero(Zf[:]).then_inc(set_up, 1)
            fill_transposed(0, 0)
            act.wait_ge(bottom_loaded, 16)
            copy(ETv[:, :, 0], Zf[:, BOTTOM, :]).then_inc(bottom_in_et, 1)
            act.wait_ge(set_up, 4)
            gram(0, 0)
            for n in range(2):
                act.wait_ge(w1_loaded[n], 16)
                copy(hi_of[N_OH + n], stage[N_OH + n]).then_inc(hi_split, 1)
            fill_transposed(0, 1)
            gram(0, 1)
            act.wait_ge(small_loaded, 4 * 16)
            rest_of_step(0)
            with act.Fori(1, CHUNKS - 1) as c:
                step(c)
            c = CHUNKS - 1
            gram(c, 0)
            gram(c, 1)
            for m in (0, 2):
                take_layer(c, m // 2, h1[:, m, :], B1[:, m:m + 1])
            take_layer(c, 2, h2[:, 0, :], B2[:, 0:1])
            take_y(c)
            act.wait_ge(y_stored, CHUNKS * 16)


def pair_rows():
    import numpy as np
    slot = {feature: n for n, feature in enumerate(SLOTS)}
    at = []
    for i, j in zip(*np.triu_indices(F, k=1)):
        a, b = sorted((slot[int(i)], slot[int(j)]))
        at.append((b % 4, a, b // 4))
    return np.array(at).T


def kernel(**inputs):
    import numpy as np
    import concourse.bacc as bacc
    from concourse import mybir as mb
    from concourse.bass_utils import run_bass_kernel_spmd

    x = {k: np.asarray(v) for k, v in inputs.items()}
    w1 = x["W_top1"]
    w1_laid = np.zeros((4, 32, KT, H1), w1.dtype)
    q, a, j = pair_rows()
    w1_laid[q, a, j] = w1[:len(q)]
    w1_laid.reshape(P, KT, H1)[:, BOTTOM] = w1[len(q):]
    laid = {
        "ids_g": x["ids"][:, GATHER],
        "ids_oh": x["ids"].T[ONEHOT],
        "bottom_t": x["r_bottom_output"].T,
        "w1": w1_laid.reshape(P, KT * H1),
        "b1": x["b_top1"].reshape(M1, P).T,
        "w2": x["W_top2"].reshape(M1, P, H2).transpose(1, 0, 2),
        "b2": x["b_top2"].reshape(M2, P).T,
        "w3": x["W_top3"].reshape(M2, P).T,
    }
    for t in range(26):
        laid[f"tbl_{t}"] = x[f"tbl_{t}"]
    nc = bacc.Bacc("TRN2", target_bir_lowering=False, num_devices=1)
    arrays, aps = {}, {}
    for name, v in laid.items():
        v = np.ascontiguousarray(v)
        arrays[f"in_{name}"] = v
        aps[name] = nc.dram_tensor(f"in_{name}", v.shape, mb.dt.from_np(v.dtype), kind="ExternalInput").ap()
    out = nc.dram_tensor("out_y", (1, BATCH), mb.dt.float32, kind="ExternalOutput").ap()
    tables = [aps.pop(f"tbl_{t}") for t in range(26)]
    program(nc, tables=tables, out=out, **aps)
    r = run_bass_kernel_spmd(nc, [arrays], core_ids=[0])
    return r.results[0]["out_y"].reshape(BATCH, 1)
```

```python
from contextlib import ExitStack

import concourse.bass as bass
from concourse import mybir

BATCH, DIM = 2048, 128
ROWS = [125000, 1250, 1000, 1250, 1250, 1000, 1250, 12500, 1000, 12500, 1000, 1250, 1000, 1000,
        12500, 1250, 1000, 12500, 1250, 1000, 12500, 1000, 1000, 1250, 12500, 1250]
ONEHOT = [2, 5, 8, 10, 12, 13]
GATHER = [t for t in range(26) if t not in ONEHOT]
N_OH, N_GA = len(ONEHOT), len(GATHER)
SLOTS = [0] + [t + 1 for t in ONEHOT] + [t + 1 for t in GATHER]
F = len(SLOTS)
FP = 32
P = 128
CHUNK = 256
CHUNKS = BATCH // CHUNK
TILES = CHUNK // P
BUFFERS = [(p, t) for p in range(2) for t in range(TILES)]
OH_ROWS = 1000
OH_P = 125
OH_K = OH_ROWS // OH_P
RING = OH_K
GROUP = 4
GROUPS = N_GA // GROUP
T_ITEMS = TILES * GROUPS
T_BANK = [2, 3, 0, 1, 2] + [0, 1, 3, 2, 0]
BANK = [m % 2 for m in range(N_OH)] + T_BANK
GRAM_BANKS = (2, 3)
PLACE = [BANK[:m].count(b) for m, b in enumerate(BANK)]
PER_BANK = [BANK.count(b) for b in range(4)]
TAKER = ["act"] * N_OH + [("dve", "act")[m % 2] for m in range(T_ITEMS)]
SG = 4
A = F - 1
GROWS = (SG - 1) * FP + A
PIECE = 8
PIECES = CHUNK // (SG * PIECE)
SAMPLES = {"dve": (0, 1), "act": (2, 3)}
PART = 64
PARTS = CHUNK // PART
RING_PARTS = 2
J = 7
KT = J + 1
H1, H2 = 512, 256
M1, M2 = H1 // P, H2 // P
BOTTOM = KT - 1

assert N_OH == 6 and N_GA % GROUP == 0 and len(T_BANK) == T_ITEMS


def program(nc, ids_g, ids_oh, bottom_t, tables, w1, b1, w2, b2, w3, out):
    f32, f32r, i32 = mybir.dt.float32, mybir.dt.float32r, mybir.dt.int32
    ALU, ACT = mybir.AluOpType, mybir.ActivationFunctionType

    with ExitStack() as ctx:
        def sb(name, shape, dt):
            return ctx.enter_context(nc.sbuf_tensor(name, shape, dt))

        def sem(name):
            return ctx.enter_context(nc.semaphore(name))

        idx = [[sb(f"idx{p}{t}", [P, N_GA], i32) for t in range(TILES)] for p in range(2)]
        E = [[sb(f"E{p}{t}", [P, N_GA, DIM], f32) for t in range(TILES)] for p in range(2)]
        ET = sb("ET", [P, CHUNK * FP], f32)
        Zf = sb("Zf", [P, RING_PARTS, J, PART], f32)
        Zbottom = sb("Zbottom", [P, CHUNK], f32)
        Zhi = sb("Zhi", [P, KT, CHUNK], f32r)
        Zlo = sb("Zlo", [P, KT, CHUNK], f32r)
        W1hi = sb("W1hi", [P, KT * H1], f32r)
        W1lo = sb("W1lo", [P, KT * H1], f32r)
        Thi = sb("Thi", [OH_P, N_OH * OH_K * DIM], f32r)
        Tlo = sb("Tlo", [OH_P, N_OH * OH_K * DIM], f32r)
        onehot = [sb(f"onehot{k}", [OH_P, CHUNK], f32r) for k in range(RING)]
        ohid = sb("ohid", [OH_P, N_OH, CHUNK], i32)
        row0_i = sb("row0_i", [OH_P, 1], i32)
        row0 = sb("row0", [OH_P, 1], f32)
        ident = sb("ident", [P, P], f32)
        W2hi = sb("W2hi", [P, M1 * H2], f32r)
        W2lo = sb("W2lo", [P, M1 * H2], f32r)
        W3 = sb("W3", [P, M2], f32)
        B1 = sb("B1", [P, M1], f32)
        B2 = sb("B2", [P, M2], f32)
        h1hi = sb("h1hi", [P, M1, CHUNK], f32r)
        h1lo = sb("h1lo", [P, M1, CHUNK], f32r)
        h2 = sb("h2", [P, M2, CHUNK], f32)
        h2w = sb("h2w", [P, CHUNK], f32)
        ones = sb("ones", [P, 1], f32)
        y = sb("y", [1, CHUNK], f32)

        def ps(name, shape):
            return ctx.enter_context(nc.psum_tensor(name, shape, f32))

        G = ps("G", [P, 4, 512])
        FB = [ps("FB0", [P, 512])[:], ps("FB1", [P, 512])[:], G[:, 0, :], G[:, 2, :]]
        MB = [ps(f"MB{b}", [P, 512]) for b in range(2)]

        idx_loaded = [[sem(f"idx_loaded{p}{t}") for t in range(TILES)] for p in range(2)]
        tiles_begun = sem("tiles_begun")
        gathered = [[sem(f"gathered{p}{t}") for t in range(TILES)] for p in range(2)]
        tables_loaded = [sem(f"table_loaded{k}") for k in range(N_OH)]
        w_loaded = [sem(f"w_loaded{n}") for n in range(4)]
        small_loaded = sem("small_loaded")
        ohid_loaded = sem("ohid_loaded")
        ohid_shifted = sem("ohid_shifted")
        bottom_loaded = sem("bottom_loaded")
        hi_split = sem("hi_split")
        lo_split = sem("lo_split")
        consts = sem("consts")
        set_up = sem("set_up")
        onehot_made = sem("onehot_made")
        onehot_used = sem("onehot_used")
        transposed = sem("transposed")
        fill_taken = [sem(f"fill_taken{b}") for b in range(4)]
        bottom_in_et = sem("bottom_in_et")
        gram_full = sem("gram_full")
        gram_taken = {e: sem(f"gram_taken_{e}") for e in SAMPLES}
        zhi_done = sem("zhi_done")
        zlo_done = sem("zlo_done")
        m_full = [sem(f"m_full{b}") for b in range(2)]
        m_taken = [sem(f"m_taken{b}") for b in range(2)]
        h1lo_done = sem("h1lo_done")
        half_weighted = sem("half_weighted")
        weighted = sem("weighted")
        y_stored = sem("y_stored")

        ETv = ET[:].rearrange("p (b f) -> p b f", f=FP)
        Ev = [E[1][t][:].rearrange("p f d -> p (f d)") for t in range(TILES)]
        TW = OH_K * DIM

        HW1, HW2 = KT * H1 // 2, M1 * H2 // 2

        def t_slot(k):
            return slice(k * TW, (k + 1) * TW)

        stage = [Ev[k // 2 % 2][0:OH_P, t_slot(k % 2)] for k in range(N_OH)] \
            + [Ev[1][:, 0:HW1]] + [v[:, HW1:HW1 + HW2] for v in Ev] + [Ev[0][:, 0:HW1]]

        def parts(table, w1, w2):
            return [table[:, t_slot(k)] for k in range(N_OH)] \
                + [w1[:, 0:HW1], w2[:, 0:HW2], w2[:, HW2:2 * HW2], w1[:, HW1:2 * HW1]]

        hi_of, lo_of = parts(Thi, W1hi, W2hi), parts(Tlo, W1lo, W2lo)
        N_CUT = len(stage)

        def first(count):
            return isinstance(count, int) and count <= 0

        def last_item(t):
            return N_OH + (t + 1) * GROUPS - 1

        def take_fill(who, eng, copy, c, m):
            if TAKER[m] != who:
                return
            if m < N_OH:
                eng.wait_ge(onehot_used, (c * N_OH + m + 1) * OH_K)
                src, dst = FB[BANK[m]][:, 0:CHUNK], ETv[:, :, 1 + m]
            else:
                t, g = divmod(m - N_OH, GROUPS)
                eng.wait_ge(transposed, c * T_ITEMS + (m - N_OH + 1))
                src = FB[BANK[m]].rearrange("p (f s) -> p s f", f=GROUP)
                f0 = 1 + N_OH + g * GROUP
                dst = ETv[:, t * P:(t + 1) * P, f0:f0 + GROUP]
            copy(dst, src).then_inc(fill_taken[BANK[m]], 1)

        def take_gram(who, eng, copy, c, x):
            h = x % 2
            eng.wait_ge(gram_full, c * PIECES + (x + 1))
            v = G[:, 2 * h:2 * h + 2, :].rearrange("p b (n w) -> p (b n) w", w=P)
            part = c * PARTS + x // 2
            if x % 2 == 0 and not first(part - 1):
                eng.wait_ge(zhi_done, part - 1)
                eng.wait_ge(zlo_done, part - 1)
            for q in range(4):
                js = [j for j in range(J) if 0 < 4 * j + q < F]
                b0, b1 = 4 * js[0] + q - 1, 4 * js[-1] + q - 1
                for s in SAMPLES[who]:
                    src = v[FP * s:FP * s + A, :, s * A + b0:s * A + b1 + 1:4]
                    s0 = x % 2 * PIECE * SG + s
                    dst = Zf[FP * q:FP * q + A, x // 2 % RING_PARTS, js[0]:js[-1] + 1,
                             s0:s0 + SG * (PIECE - 1) + 1:SG]
                    last = copy(dst, src.rearrange("p n j -> p j n"))
            last.then_inc(gram_taken[who], 1)

        block = ctx.enter_context(nc.Block())

        @block.sync
        def _(sp):
            for n, (p, t) in enumerate(BUFFERS):
                sp.dma_start(idx[p][t][:], ids_g[n * P:(n + 1) * P, :]).then_inc(idx_loaded[p][t], 16)
            sp.dma_start(ohid[:], ids_oh[:, 0:CHUNK].partition_broadcast(OH_P)).then_inc(ohid_loaded, 16)
            for k in range(N_OH):
                if k >= 4:
                    sp.wait_ge(lo_split, k - 3)
                sp.dma_start(stage[k], tables[ONEHOT[k]].rearrange("(p k) d -> p (k d)", k=OH_K))\
                    .then_inc(tables_loaded[k], 16)
                if k == 3:
                    for n in range(2):
                        sp.dma_start(stage[N_OH + 1 + n], w2[:, n * HW2:(n + 1) * HW2])\
                            .then_inc(w_loaded[1 + n], 16)
                    sp.dma_start(Zbottom[:], bottom_t[:, 0:CHUNK]).then_inc(bottom_loaded, 16)
            for n, cut, word in ((0, 4, 0), (3, N_OH, HW1)):
                sp.wait_ge(lo_split, cut)
                sp.dma_start(stage[N_OH + n], w1[:, word:word + HW1]).then_inc(w_loaded[n], 16)
            sp.dma_start(W3[:], w3).then_inc(small_loaded, 16)
            sp.dma_start(B1[:], b1).then_inc(small_loaded, 16)
            sp.dma_start(B2[:], b2).then_inc(small_loaded, 16)

            def load_chunk(c, p=None, i=None):
                sp.wait_ge(onehot_made, c * (N_OH * OH_K))
                sp.dma_start(ohid[:], ids_oh[:, bass.ds(c * CHUNK, CHUNK)].partition_broadcast(OH_P))\
                    .then_inc(ohid_loaded, 16)
                if p is not None:
                    for t in range(TILES):
                        sp.wait_ge(gathered[p][t], i * (16 * N_GA))
                        sp.dma_start(idx[p][t][:], ids_g[CHUNK + t * P:, :][bass.ds(c * CHUNK, P), :])\
                            .then_inc(idx_loaded[p][t], 16)
                sp.wait_ge(zhi_done, c * PARTS)
                sp.wait_ge(zlo_done, c * PARTS)
                sp.dma_start(Zbottom[:], bottom_t[:, bass.ds(c * CHUNK, CHUNK)])\
                    .then_inc(bottom_loaded, 16)

            with sp.Fori(0, CHUNKS // 2 - 1) as i:
                load_chunk(i * 2 + 1, 0, i + 1)
                load_chunk(i * 2 + 2, 1, i + 1)
            load_chunk(CHUNKS - 1)

        @block.gpsimd
        def _(pool):
            nc.gpsimd.iota(row0_i[:], pattern=[[0, 1]], base=0, channel_multiplier=OH_K)\
                .then_inc(consts, 1)
            nc.gpsimd.memset(ident[:], 0.0).then_inc(consts, 1)
            pool.wait_ge(consts, 2)
            nc.gpsimd.affine_select(out=ident[:], in_=ident[:], compare_op=ALU.not_equal, fill=1.0,
                                    base=0, pattern=[[-1, P]], channel_multiplier=1).then_inc(consts, 1)

            def gather(p, t):
                for k, table in enumerate(GATHER):
                    pool.indirect_dma_start(
                        E[p][t][:, k, :], None, tables[table],
                        bass.IndirectOffsetOnAxis(ap=idx[p][t][:, k:k + 1], axis=0))\
                        .then_inc(gathered[p][t], 16)

            for p, t in BUFFERS:
                pool.wait_ge(idx_loaded[p][t], 16)
                if p:
                    pool.wait_ge(lo_split, N_CUT)
                gather(p, t)
            with pool.Fori(1, CHUNKS // 2) as i:
                for p, t in BUFFERS:
                    pool.wait_ge(idx_loaded[p][t], (i + 1) * 16)
                    pool.wait_ge(transposed, i * (2 * T_ITEMS) + ((p - 2) * T_ITEMS + (t + 1) * GROUPS))
                    pool.sem_inc(tiles_begun)
                    gather(p, t)

        @block.tensor
        def _(pe):
            def free_bank(c, m):
                if not first(c * PER_BANK[BANK[m]] + PLACE[m]):
                    pe.wait_ge(fill_taken[BANK[m]], c * PER_BANK[BANK[m]] + PLACE[m])

            def fill_onehot(c):
                for k in range(N_OH):
                    o = FB[BANK[k]][:, 0:CHUNK]
                    free_bank(c, k)
                    if first(c):
                        pe.wait_ge(lo_split, k + 1)
                    for kt in range(OH_K):
                        pe.wait_ge(onehot_made, (c * N_OH + k) * OH_K + (kt + 1))
                        w = slice(k * TW + kt * DIM, k * TW + (kt + 1) * DIM)
                        nc.tensor.matmul(o, Thi[:, w], onehot[kt][:], start=(kt == 0), stop=False)
                        nc.tensor.matmul(o, Tlo[:, w], onehot[kt][:], start=False,
                                         stop=(kt == OH_K - 1)).then_inc(onehot_used, 1)

            def fill_transposed(c, p, i, t):
                pe.wait_ge(gathered[p][t], (i + 1) * (16 * N_GA))
                for g in range(GROUPS):
                    m = N_OH + t * GROUPS + g
                    if t == 1 and BANK[m] in GRAM_BANKS:
                        for who in SAMPLES:
                            pe.wait_ge(gram_taken[who], c * PIECES + PIECES // TILES)
                    free_bank(c, m)
                    for f in range(GROUP):
                        last = nc.tensor.transpose(FB[BANK[m]][:, f * P:(f + 1) * P],
                                                   E[p][t][:, g * GROUP + f, :], ident[:])
                    last.then_inc(transposed, 1)

            def gram(c, t):
                pe.wait_ge(bottom_in_et, c + 1)
                for b in range(4):
                    pe.wait_ge(fill_taken[b], c * PER_BANK[b] + BANK[:last_item(t) + 1].count(b))
                for x in range(t * PIECES // TILES, (t + 1) * PIECES // TILES):
                    h = x % 2
                    if not first(c * PIECES + (x - 1)):
                        pe.wait_ge(gram_taken["dve"], c * PIECES + (x - 1))
                        pe.wait_ge(gram_taken["act"], c * PIECES + (x - 1))
                    for n in range(PIECE):
                        s0 = (x * PIECE + n) * SG
                        last = nc.tensor.matmul(
                            G[0:GROWS, 2 * h + n // 4, (n % 4) * P:(n % 4) * P + SG * A],
                            ET[:, s0 * FP:s0 * FP + GROWS], ETv[:, s0:s0 + SG, 1:F],
                            start=True, stop=True)
                    last.then_inc(gram_full, 1)

            def top1(c, quarters):
                pe.wait_ge(zhi_done, (c + 1) * PARTS)
                for m in quarters:
                    b = m % 2
                    if not first(c * (4 - b) + m // 2):
                        pe.wait_ge(m_taken[b], c * (4 - b) + m // 2)
                    o = MB[b][:, 0:CHUNK]
                    for k in range(KT):
                        w = slice(k * H1 + m * P, k * H1 + (m + 1) * P)
                        nc.tensor.matmul(o, W1hi[:, w], Zhi[:, k, :], start=(k == 0), stop=False)
                        nc.tensor.matmul(o, W1lo[:, w], Zhi[:, k, :], start=False, stop=False)
                    if m == 0:
                        pe.wait_ge(zlo_done, (c + 1) * PARTS)
                    for k in range(KT):
                        w = slice(k * H1 + m * P, k * H1 + (m + 1) * P)
                        last = nc.tensor.matmul(o, W1hi[:, w], Zlo[:, k, :], start=False,
                                                stop=(k == KT - 1))
                    last.then_inc(m_full[b], 1)

            def top2(c, m):
                for k in range(M1):
                    if m == 0 and k == 0:
                        pe.wait_ge(m_taken[0], c * 4 + 2)
                    if m == 0 and k % 2:
                        pe.wait_ge(m_taken[1], c * 3 + (k + 1) // 2)
                    w = slice(k * H2 + m * P, k * H2 + (m + 1) * P)
                    o = MB[m][:, 0:CHUNK]
                    nc.tensor.matmul(o, W2hi[:, w], h1hi[:, k, :], start=(k == 0), stop=False)
                    nc.tensor.matmul(o, W2lo[:, w], h1hi[:, k, :], start=False, stop=False)
                    if m == 0:
                        pe.wait_ge(h1lo_done, c * M1 + (k + 1))
                    last = nc.tensor.matmul(o, W2hi[:, w], h1lo[:, k, :], start=False,
                                            stop=(k == M1 - 1))
                last.then_inc(m_full[m], 1)

            def top3(c):
                pe.wait_ge(weighted, c + 1)
                nc.tensor.matmul(MB[0][0:1, 0:CHUNK], ones[:], h2w[:], start=True, stop=True)\
                    .then_inc(m_full[0], 1)

            def step(c, p_next, i_next):
                gram(c, 1)
                if not first(c):
                    top3(c - 1)
                fill_onehot(c + 1)
                if first(c):
                    pe.wait_ge(lo_split, N_CUT)
                top1(c, range(M1 - 1))
                fill_transposed(c + 1, p_next, i_next, 0)
                top1(c, [M1 - 1])
                gram(c + 1, 0)
                top2(c, 0)
                fill_transposed(c + 1, p_next, i_next, 1)
                top2(c, 1)

            pe.wait_ge(consts, 3)
            fill_onehot(0)
            fill_transposed(0, 0, 0, 0)
            gram(0, 0)
            fill_transposed(0, 0, 0, 1)
            step(0, 1, 0)
            with pe.Fori(0, CHUNKS // 2 - 1) as i:
                step(i * 2 + 1, 0, i + 1)
                step(i * 2 + 2, 1, i + 1)
            c = CHUNKS - 1
            gram(c, 1)
            top3(c - 1)
            top1(c, range(M1))
            top2(c, 0)
            top2(c, 1)
            top3(c)

        @block.vector
        def _(dve):
            def copy(dst, src):
                return nc.vector.tensor_copy(dst, src)

            def make_onehot(c, k):
                for kt in range(OH_K):
                    if not first((c * N_OH + k) * OH_K):
                        dve.wait_ge(onehot_used, (c * N_OH + (k - 1)) * OH_K + (kt + 1))
                    nc.vector.tensor_single_scalar(onehot[kt][:], ohid[:, k, :].bitcast(f32), float(kt),
                                                   ALU.is_equal).then_inc(onehot_made, 1)

            def lo_part(lo, full, hi):
                return nc.vector.tensor_tensor(lo, full, hi.bitcast(f32), ALU.subtract)

            def first_onehot(c):
                dve.wait_ge(ohid_loaded, (c + 1) * 16)
                nc.vector.tensor_scalar(ohid[:].bitcast(f32), ohid[:], row0[:], None, ALU.subtract)\
                    .then_inc(ohid_shifted, 1)
                dve.wait_ge(ohid_shifted, c + 1)
                make_onehot(c, 0)

            def fill_transposed(c, t):
                for m in range(N_OH + t * GROUPS, N_OH + (t + 1) * GROUPS):
                    take_fill("dve", dve, copy, c, m)

            def take_layer(c, n, dst, bias):
                dve.wait_ge(m_full[1], c * 3 + (n + 1))
                nc.vector.tensor_scalar(dst, MB[1][:, 0:CHUNK], bias, 0.0, ALU.add, ALU.max)\
                    .then_inc(m_taken[1], 1)

            def take_h1(c, n):
                m = 2 * n + 1
                dve.wait_ge(m_full[1], c * 3 + (n + 1))
                if n:
                    dve.wait_ge(h1lo_done, c * M1 + 2)
                for dst in (h1hi[:, m, :], h2[:, 1, :]):
                    last = nc.vector.tensor_scalar(dst, MB[1][:, 0:CHUNK], B1[:, m:m + 1], 0.0,
                                                   ALU.add, ALU.max)
                last.then_inc(m_taken[1], 1)

            def cut_h1(c, m):
                dve.wait_ge(m_taken[m % 2], c * (4 - m % 2) + (m // 2 + 1))
                lo_part(h1lo[:, m, :], h2[:, m % 2, :], h1hi[:, m, :]).then_inc(h1lo_done, 1)

            def take_h2(c):
                dve.wait_ge(m_taken[0], c * 4 + 3)
                nc.vector.tensor_scalar(h2w[:], h2[:, 0, :], W3[:, 0:1], None, ALU.mult)\
                    .then_inc(half_weighted, 1)
                take_layer(c, 2, h2[:, 1, :], B2[:, 1:2])
                dve.wait_ge(m_taken[1], c * 3 + 3)
                dve.wait_ge(half_weighted, c + 1)
                nc.vector.scalar_tensor_tensor(h2w[:], h2[:, 1, :], W3[:, 1:2], h2w[:],
                                               ALU.mult, ALU.add).then_inc(weighted, 1)

            def cut_lo(c, r):
                at = slice(r * PART, (r + 1) * PART)
                dve.wait_ge(zhi_done, c * PARTS + (r + 1))
                if r == 0:
                    lo_part(Zlo[:, BOTTOM, :], Zbottom[:], Zhi[:, BOTTOM, :])
                lo_part(Zlo[:, 0:J, at], Zf[:, r % RING_PARTS], Zhi[:, 0:J, at]).then_inc(zlo_done, 1)

            def gram(c, t):
                for x in range(t * PIECES // TILES, (t + 1) * PIECES // TILES):
                    take_gram("dve", dve, copy, c, x)
                    if x % 2 == 0 and x:
                        cut_lo(c, x // 2 - 1)

            def step(c, more=True):
                gram(c, 1)
                for k in range(1, N_OH):
                    make_onehot(c + 1, k)
                cut_lo(c, PARTS - 1)
                if more:
                    first_onehot(c + 2)
                cut_h1(c, 0)
                take_h1(c, 0)
                cut_h1(c, 1)
                fill_transposed(c + 1, 0)
                cut_h1(c, 2)
                take_h1(c, 1)
                cut_h1(c, 3)
                gram(c + 1, 0)
                fill_transposed(c + 1, 1)
                take_h2(c)

            def cut(k):
                dve.wait_ge(hi_split, k + 1)
                lo_part(lo_of[k], stage[k], hi_of[k]).then_inc(lo_split, 1)

            dve.wait_ge(consts, 3)
            nc.vector.tensor_copy(row0[:], row0_i[:]).then_inc(set_up, 1)
            nc.vector.memset(ones[:], 1.0).then_inc(set_up, 1)
            nc.vector.memset(ETv[:, :, F:FP], 0.0).then_inc(set_up, 1)
            dve.wait_ge(set_up, 4)
            first_onehot(0)
            for k in range(N_OH):
                cut(k)
                if k:
                    make_onehot(0, k)
            for k in range(N_OH, N_CUT - 1):
                cut(k)
            fill_transposed(0, 0)
            gram(0, 0)
            cut(N_CUT - 1)
            first_onehot(1)
            fill_transposed(0, 1)
            dve.wait_ge(small_loaded, 3 * 16)
            step(0)
            with dve.Fori(1, CHUNKS - 2) as c:
                step(c)
            step(CHUNKS - 2, more=False)
            c = CHUNKS - 1
            gram(c, 1)
            cut_lo(c, PARTS - 1)
            for n in range(2):
                cut_h1(c, 2 * n)
                take_h1(c, n)
                cut_h1(c, 2 * n + 1)
            take_h2(c)

        @block.scalar
        def _(act):
            def copy(dst, src):
                return nc.scalar.activation(dst, src, ACT.Copy)

            def fill_onehot(c):
                for k in range(N_OH):
                    take_fill("act", act, copy, c, k)
                act.wait_ge(bottom_loaded, (c + 1) * 16)
                copy(ETv[:, :, 0], Zbottom[:]).then_inc(bottom_in_et, 1)

            def fill_transposed(c, t):
                for m in range(N_OH + t * GROUPS, N_OH + (t + 1) * GROUPS):
                    take_fill("act", act, copy, c, m)

            def take_layer(c, n, dst, bias):
                act.wait_ge(m_full[0], c * 4 + (n + 1))
                nc.scalar.activation(dst, MB[0][:, 0:CHUNK], ACT.Relu, bias=bias)\
                    .then_inc(m_taken[0], 1)

            def gram(c, t):
                for x in range(t * PIECES // TILES, (t + 1) * PIECES // TILES):
                    take_gram("act", act, copy, c, x)
                    if x % 2:
                        for who in SAMPLES:
                            act.wait_ge(gram_taken[who], c * PIECES + (x + 1))
                        at = slice(x // 2 * PART, (x // 2 + 1) * PART)
                        if x == 1:
                            copy(Zhi[:, BOTTOM, :], Zbottom[:])
                        copy(Zhi[:, 0:J, at], Zf[:, x // 2 % RING_PARTS]).then_inc(zhi_done, 1)

            def take_h1(c, n):
                m = 2 * n
                act.wait_ge(m_full[0], c * 4 + (n + 1))
                if n:
                    act.wait_ge(h1lo_done, c * M1 + 1)
                for dst in (h1hi[:, m, :], h2[:, 0, :]):
                    last = nc.scalar.activation(dst, MB[0][:, 0:CHUNK], ACT.Relu, bias=B1[:, m:m + 1])
                last.then_inc(m_taken[0], 1)

            def take_y(c):
                act.wait_ge(m_full[0], c * 4 + 4)
                copy(y[:], MB[0][0:1, 0:CHUNK]).then_inc(m_taken[0], 1)
                act.wait_ge(m_taken[0], c * 4 + 4)
                act.dma_start(out[:, bass.ds(c * CHUNK, CHUNK)], y[:]).then_inc(y_stored, 16)

            def step(c):
                gram(c, 1)
                if not first(c):
                    take_y(c - 1)
                fill_onehot(c + 1)
                take_h1(c, 0)
                take_h1(c, 1)
                fill_transposed(c + 1, 0)
                gram(c + 1, 0)
                take_layer(c, 2, h2[:, 0, :], B2[:, 0:1])
                fill_transposed(c + 1, 1)
                if not first(c):
                    act.wait_ge(y_stored, c * 16)

            def cut(k, loaded):
                act.wait_ge(loaded, 16)
                copy(hi_of[k], stage[k]).then_inc(hi_split, 1)

            nc.scalar.memzero(Zf[:]).then_inc(set_up, 1)
            act.wait_ge(set_up, 4)
            for k in range(N_OH):
                cut(k, tables_loaded[k])
                if k:
                    take_fill("act", act, copy, 0, k - 1)
            for n in range(3):
                cut(N_OH + n, w_loaded[n])
            take_fill("act", act, copy, 0, N_OH - 1)
            fill_transposed(0, 0)
            act.wait_ge(bottom_loaded, 16)
            copy(ETv[:, :, 0], Zbottom[:]).then_inc(bottom_in_et, 1)
            gram(0, 0)
            cut(N_CUT - 1, w_loaded[3])
            fill_transposed(0, 1)
            act.wait_ge(small_loaded, 3 * 16)
            step(0)
            with act.Fori(1, CHUNKS - 1) as c:
                step(c)
            c = CHUNKS - 1
            gram(c, 1)
            take_y(c - 1)
            take_h1(c, 0)
            take_h1(c, 1)
            take_layer(c, 2, h2[:, 0, :], B2[:, 0:1])
            act.wait_ge(y_stored, c * 16)
            take_y(c)
            act.wait_ge(y_stored, CHUNKS * 16)


def pair_rows():
    import numpy as np
    slot = {feature: n for n, feature in enumerate(SLOTS)}
    at = []
    for i, j in zip(*np.triu_indices(F, k=1)):
        a, b = sorted((slot[int(i)], slot[int(j)]))
        at.append((b % 4, a, b // 4))
    return np.array(at).T


def kernel(**inputs):
    import numpy as np
    import concourse.bacc as bacc
    from concourse import mybir as mb
    from concourse.bass_utils import run_bass_kernel_spmd

    x = {k: np.asarray(v) for k, v in inputs.items()}
    w1 = x["W_top1"]
    w1_laid = np.zeros((4, 32, KT, H1), w1.dtype)
    q, a, j = pair_rows()
    w1_laid[q, a, j] = w1[:len(q)]
    w1_laid.reshape(P, KT, H1)[:, BOTTOM] = w1[len(q):]
    laid = {
        "ids_g": x["ids"][:, GATHER],
        "ids_oh": x["ids"].T[ONEHOT],
        "bottom_t": x["r_bottom_output"].T,
        "w1": w1_laid.reshape(P, KT * H1),
        "b1": x["b_top1"].reshape(M1, P).T,
        "w2": x["W_top2"].reshape(M1, P, H2).transpose(1, 0, 2).reshape(P, M1 * H2),
        "b2": x["b_top2"].reshape(M2, P).T,
        "w3": x["W_top3"].reshape(M2, P).T,
    }
    for t in range(26):
        laid[f"tbl_{t}"] = x[f"tbl_{t}"]
    nc = bacc.Bacc("TRN2", target_bir_lowering=False, num_devices=1)
    arrays, aps = {}, {}
    for name, v in laid.items():
        v = np.ascontiguousarray(v)
        arrays[f"in_{name}"] = v
        aps[name] = nc.dram_tensor(f"in_{name}", v.shape, mb.dt.from_np(v.dtype), kind="ExternalInput").ap()
    out = nc.dram_tensor("out_y", (1, BATCH), mb.dt.float32, kind="ExternalOutput").ap()
    tables = [aps.pop(f"tbl_{t}") for t in range(26)]
    program(nc, tables=tables, out=out, **aps)
    r = run_bass_kernel_spmd(nc, [arrays], core_ids=[0])
    return r.results[0]["out_y"].reshape(BATCH, 1)
```
